# Optimizing a Trainium2 kernel written in Bass

```python
import numpy as np
import jax
import jax.numpy as jnp

def _softmax(x, axis=-1):
    return jax.nn.softmax(x, axis=axis)

def _gelu(x):
    return jax.nn.gelu(x, approximate=True)

def _silu(x):
    return jax.nn.silu(x)

def _sigmoid(x):
    return jax.nn.sigmoid(x)

def _layernorm(x, axis=-1, eps=1e-05):
    m = jnp.mean(x, axis=axis, keepdims=True)
    v = jnp.var(x, axis=axis, keepdims=True)
    return (x - m) / jnp.sqrt(v + eps)

def _scatter_add(tgt, idx, src, axis=0):
    return tgt.at[idx].add(src)

def _segment_sum(src, seg, n):
    return jax.ops.segment_sum(src, seg, n)
kernel_name = 'mk_gnn_preln_d4_gnn_r8_489452'

def setup_inputs(seed: int=0):
    np.random.seed(seed)
    _w = jnp.asarray

    def _rec_inputs():
        import jax
        import jax.numpy as jnp
        _gk = jax.random.key(seed)
        x = -0.0003713 + 1 * jax.random.normal(jax.random.fold_in(_gk, 1), (6250, 128), jnp.float32)
        src = jax.random.randint(jax.random.fold_in(_gk, 2), (100000,), 0, 6250, jnp.int32)
        dst = jnp.minimum((6250 * jax.random.uniform(jax.random.fold_in(_gk, 3), (100000,)) ** 2.0).astype(jnp.int32), 49999)
        _o = jnp.argsort(dst, stable=True)
        src = src[_o]
        dst = dst[_o]
        edge_attr_4 = 0.0012443 + 1.0001 * jax.random.normal(jax.random.fold_in(_gk, 12), (100000, 4), jnp.float32)
        edge_attr_64 = 0.000196303 + 1.00016 * jax.random.normal(jax.random.fold_in(_gk, 13), (100000, 64), jnp.float32)
        edge_attr_8 = -0.000521468 + 0.999954 * jax.random.normal(jax.random.fold_in(_gk, 14), (100000, 8), jnp.float32)
        edge_weight = jax.random.uniform(jax.random.fold_in(_gk, 16), (100000,), jnp.float32, 0.0, 0.999998)
        node_vec1 = jax.random.uniform(jax.random.fold_in(_gk, 17), (6250, 1), jnp.float32, 0.0, 1)
        return (x, src, dst, edge_attr_4, edge_attr_64, edge_attr_8, edge_weight, node_vec1)
    x, src, dst, edge_attr_4, edge_attr_64, edge_attr_8, edge_weight, node_vec1 = _rec_inputs()

    def _L0_gnn_setup():
        import jax, jax.numpy as jnp
        import numpy as np
        BN_EPS = 1e-05
        key = jax.random.key(seed)
        k_x, k_idx, k_val, k_w = jax.random.split(key, 4)
        n_nodes, nnz, d_in, d_out = (12500, 100000, 128, 128)
        x = jax.random.normal(k_x, (n_nodes, d_in), dtype=jnp.float32)
        A_indices = jax.random.randint(k_idx, (2, nnz), 0, n_nodes, dtype=jnp.int64)
        A_values = jax.random.uniform(k_val, (nnz,), dtype=jnp.float32)
        W = jax.random.normal(k_w, (d_out, d_in), dtype=jnp.float32) / np.sqrt(d_in)
        gamma = jnp.ones((d_out,), dtype=jnp.float32)
        beta = jnp.zeros((d_out,), dtype=jnp.float32)
        return {'x': x, 'A_indices': A_indices, 'A_values': A_values, 'W': W, 'gamma': gamma, 'beta': beta, 'm': n_nodes, 'n': n_nodes}
    _L0_gnn_all = _L0_gnn_setup()
    _L0_gnn_in = {k: v for k, v in _L0_gnn_all.items() if k in ('W', 'gamma', 'beta')}
    del _L0_gnn_all

    def _L1_gnn_setup():
        import jax, jax.numpy as jnp
        import numpy as np
        N_NODES = 12500
        N_EDGES = 200000
        DIM = 128
        key = jax.random.key(seed)
        k_x, k_e, k_wm, k_bm, k_wu, k_bu = jax.random.split(key, 6)
        bound = 1.0 / np.sqrt(DIM)
        return {'x': jax.random.normal(k_x, (N_NODES, DIM), dtype=jnp.float32), 'edge_index': jax.random.randint(k_e, (2, N_EDGES), 0, N_NODES, dtype=jnp.int64), 'W_msg': jax.random.uniform(k_wm, (DIM, DIM), jnp.float32, -bound, bound), 'b_msg': jax.random.uniform(k_bm, (DIM,), jnp.float32, -bound, bound), 'W_upd': jax.random.uniform(k_wu, (DIM, DIM), jnp.float32, -bound, bound), 'b_upd': jax.random.uniform(k_bu, (DIM,), jnp.float32, -bound, bound)}
    _L1_gnn_all = _L1_gnn_setup()
    _L1_gnn_in = {k: v for k, v in _L1_gnn_all.items() if k in ('W_msg', 'b_msg', 'W_upd', 'b_upd')}
    del _L1_gnn_all

    def _L2_gnn_setup():
        import jax, jax.numpy as jnp
        import numpy as np
        N, E = (6250, 50000)
        NODE_DIM, EDGE_DIM = (128, 64)
        MSG_IN = 2 * NODE_DIM + EDGE_DIM
        key = jax.random.key(seed)
        ks = jax.random.split(key, 12)
        h = jax.random.normal(ks[0], (N, NODE_DIM), dtype=jnp.float32)
        edge_index = jax.random.randint(ks[1], (2, E), 0, N, dtype=jnp.int64)
        e = jax.random.normal(ks[2], (E, EDGE_DIM), dtype=jnp.float32)

        def lin(k, fan_in, fan_out):
            bound = 1.0 / np.sqrt(fan_in)
            k1, k2 = jax.random.split(k)
            w = jax.random.uniform(k1, (fan_in, fan_out), minval=-bound, maxval=bound, dtype=jnp.float32)
            b = jax.random.uniform(k2, (fan_out,), minval=-bound, maxval=bound, dtype=jnp.float32)
            return (w, b)
        w1, b1 = lin(ks[3], MSG_IN, NODE_DIM)
        w2, b2 = lin(ks[4], NODE_DIM, NODE_DIM)
        wg, bg = lin(ks[5], MSG_IN, NODE_DIM)
        wu, bu = lin(ks[6], 2 * NODE_DIM, NODE_DIM)
        return {'h': h, 'edge_index': edge_index, 'e': e, 'w1': w1, 'b1': b1, 'w2': w2, 'b2': b2, 'wg': wg, 'bg': bg, 'wu': wu, 'bu': bu}
    _L2_gnn_all = _L2_gnn_setup()
    _L2_gnn_in = {k: v for k, v in _L2_gnn_all.items() if k in ('w1', 'b1', 'w2', 'b2', 'wg', 'bg', 'wu', 'bu')}
    del _L2_gnn_all

    def _L3_gnn_setup():
        import jax, jax.numpy as jnp
        import numpy as np
        N_NODES = 5000
        N_EDGES = 80000
        MUL = 32
        NUM_NEIGHBORS = 16.0
        SILU_NORM = 1.6791767923989418
        SQRT3 = 3.0 ** 0.5
        key = jax.random.key(seed)
        ks = jax.random.split(key, 12)
        return {'node_input': jax.random.normal(ks[0], (N_NODES, 4 * MUL), dtype=jnp.float32), 'node_attr': jnp.ones((N_NODES, 1), dtype=jnp.float32), 'edge_src': jax.random.randint(ks[1], (N_EDGES,), 0, N_NODES, dtype=jnp.int32), 'edge_dst': jax.random.randint(ks[2], (N_EDGES,), 0, N_NODES, dtype=jnp.int32), 'edge_attr': jax.random.normal(ks[3], (N_EDGES, 4), dtype=jnp.float32), 'edge_scalars': jax.random.normal(ks[4], (N_EDGES, 8), dtype=jnp.float32), 'w_lin1_s': jax.random.normal(ks[5], (MUL, MUL), dtype=jnp.float32), 'w_lin1_v': jax.random.normal(ks[6], (MUL, MUL), dtype=jnp.float32), 'fc_w1': jax.random.normal(ks[7], (8, 64), dtype=jnp.float32), 'fc_w2': jax.random.normal(ks[8], (64, 4 * MUL), dtype=jnp.float32), 'w_lin2_s': jax.random.normal(ks[9], (2 * MUL, MUL), dtype=jnp.float32), 'w_lin2_v': jax.random.normal(ks[10], (2 * MUL, MUL), dtype=jnp.float32)}
    _L3_gnn_all = _L3_gnn_setup()
    _L3_gnn_in = {k: v for k, v in _L3_gnn_all.items() if k in ('w_lin1_s', 'w_lin1_v', 'fc_w1', 'fc_w2', 'w_lin2_s', 'w_lin2_v')}
    del _L3_gnn_all
    return {'x': x, 'src': src, 'dst': dst, 'edge_attr_4': edge_attr_4, 'edge_attr_64': edge_attr_64, 'edge_attr_8': edge_attr_8, 'edge_weight': edge_weight, 'node_vec1': node_vec1, 'L0_gnn_W': _L0_gnn_in['W'], 'L0_gnn_gamma': _L0_gnn_in['gamma'], 'L0_gnn_beta': _L0_gnn_in['beta'], 'L1_gnn_W_msg': _L1_gnn_in['W_msg'], 'L1_gnn_b_msg': _L1_gnn_in['b_msg'], 'L1_gnn_W_upd': _L1_gnn_in['W_upd'], 'L1_gnn_b_upd': _L1_gnn_in['b_upd'], 'L2_gnn_w1': _L2_gnn_in['w1'], 'L2_gnn_b1': _L2_gnn_in['b1'], 'L2_gnn_w2': _L2_gnn_in['w2'], 'L2_gnn_b2': _L2_gnn_in['b2'], 'L2_gnn_wg': _L2_gnn_in['wg'], 'L2_gnn_bg': _L2_gnn_in['bg'], 'L2_gnn_wu': _L2_gnn_in['wu'], 'L2_gnn_bu': _L2_gnn_in['bu'], 'L3_gnn_w_lin1_s': _L3_gnn_in['w_lin1_s'], 'L3_gnn_w_lin1_v': _L3_gnn_in['w_lin1_v'], 'L3_gnn_fc_w1': _L3_gnn_in['fc_w1'], 'L3_gnn_fc_w2': _L3_gnn_in['fc_w2'], 'L3_gnn_w_lin2_s': _L3_gnn_in['w_lin2_s'], 'L3_gnn_w_lin2_v': _L3_gnn_in['w_lin2_v']}

def reference(x, src, dst, edge_attr_4, edge_attr_64, edge_attr_8, edge_weight, node_vec1, L0_gnn_W, L0_gnn_gamma, L0_gnn_beta, L1_gnn_W_msg, L1_gnn_b_msg, L1_gnn_W_upd, L1_gnn_b_upd, L2_gnn_w1, L2_gnn_b1, L2_gnn_w2, L2_gnn_b2, L2_gnn_wg, L2_gnn_bg, L2_gnn_wu, L2_gnn_bu, L3_gnn_w_lin1_s, L3_gnn_w_lin1_v, L3_gnn_fc_w1, L3_gnn_fc_w2, L3_gnn_w_lin2_s, L3_gnn_w_lin2_v):
    import jax
    import jax.numpy as jnp

    def _L0_gnn_ref(x, A_indices, A_values, W, gamma, beta, m, n):
        import jax, jax.numpy as jnp
        import numpy as np
        BN_EPS = 1e-05
        rows, cols = (A_indices[0], A_indices[1])
        gathered = x[cols] * A_values[:, None]
        h = jax.ops.segment_sum(gathered, rows, num_segments=m)
        h = jnp.einsum('md,od->mo', h, W)
        mean = jnp.mean(h, axis=0)
        var = jnp.var(h, axis=0)
        h = (h - mean) * jax.lax.rsqrt(var + BN_EPS) * gamma + beta
        return jax.nn.relu(h)

    def _L1_gnn_ref(x, edge_index, W_msg, b_msg, W_upd, b_upd):
        import jax, jax.numpy as jnp
        import numpy as np
        N_NODES = 12500
        N_EDGES = 200000
        DIM = 128
        messages = jax.nn.relu(x @ W_msg.T + b_msg)
        src, dst = (edge_index[0], edge_index[1])
        aggregated = jax.ops.segment_sum(messages[src], dst, num_segments=x.shape[0])
        updated = jax.nn.relu(aggregated @ W_upd.T + b_upd)
        return updated + x

    def _L2_gnn_ref(h, edge_index, e, w1, b1, w2, b2, wg, bg, wu, bu):
        import jax, jax.numpy as jnp
        import numpy as np
        N, E = (6250, 50000)
        NODE_DIM, EDGE_DIM = (128, 64)
        MSG_IN = 2 * NODE_DIM + EDGE_DIM
        src, dst = (edge_index[0], edge_index[1])
        msg_in = jnp.concatenate([h[src], h[dst], e], axis=-1)
        messages = jax.nn.silu(msg_in @ w1 + b1) @ w2 + b2
        gates = jax.nn.sigmoid(msg_in @ wg + bg)
        messages = messages * gates
        n = h.shape[0]
        agg = jax.ops.segment_sum(messages, dst, num_segments=n)
        deg = jax.ops.segment_sum(jnp.ones((dst.shape[0],), h.dtype), dst, num_segments=n)
        agg = agg / jnp.maximum(deg, 1.0)[:, None]
        h_new = jax.nn.silu(jnp.concatenate([h, agg], axis=-1) @ wu + bu)
        return h_new

    def _L3_gnn_ref(node_input, node_attr, edge_src, edge_dst, edge_attr, edge_scalars, w_lin1_s, w_lin1_v, fc_w1, fc_w2, w_lin2_s, w_lin2_v):
        import jax, jax.numpy as jnp
        import numpy as np
        N_NODES = 5000
        N_EDGES = 80000
        MUL = 32
        NUM_NEIGHBORS = 16.0
        SILU_NORM = 1.6791767923989418
        SQRT3 = 3.0 ** 0.5
        N = node_input.shape[0]
        s = node_input[:, :MUL]
        v = node_input[:, MUL:].reshape(N, MUL, 3)
        s = s @ (w_lin1_s / jnp.sqrt(jnp.float32(MUL)))
        v = jnp.einsum('nui,uw->nwi', v, w_lin1_v / jnp.sqrt(jnp.float32(MUL)))
        h = jax.nn.silu(edge_scalars @ (fc_w1 / jnp.sqrt(jnp.float32(fc_w1.shape[0])))) * SILU_NORM
        w = h @ (fc_w2 / jnp.sqrt(jnp.float32(fc_w2.shape[0])))
        w0 = w[:, 0 * MUL:1 * MUL]
        w1 = w[:, 1 * MUL:2 * MUL]
        w2 = w[:, 2 * MUL:3 * MUL]
        w3 = w[:, 3 * MUL:4 * MUL]
        se = s[edge_src]
        ve = v[edge_src]
        es = edge_attr[:, :1]
        ev = edge_attr[:, 1:4]
        mid_s0 = w0 * se * es
        mid_s1 = w3 * jnp.einsum('eui,ei->eu', ve, ev) / SQRT3
        mid_v0 = (w1 * se)[:, :, None] * ev[:, None, :]
        mid_v1 = (w2 * es)[:, :, None] * ve
        mid_scal = jnp.concatenate([mid_s0, mid_s1], axis=1)
        mid_vec = jnp.concatenate([mid_v0, mid_v1], axis=1)
        inv = 1.0 / jnp.sqrt(jnp.float32(NUM_NEIGHBORS))
        ns = jax.ops.segment_sum(mid_scal, edge_dst, num_segments=N) * inv
        nv = jax.ops.segment_sum(mid_vec, edge_dst, num_segments=N) * inv
        fan = jnp.sqrt(jnp.float32(2 * MUL))
        out_s = ns @ (w_lin2_s / fan)
        out_v = jnp.einsum('nui,uw->nwi', nv, w_lin2_v / fan)
        return jnp.concatenate([out_s, out_v.reshape(N, -1)], axis=1)
    edge_index = jnp.stack([src, dst])
    h = jnp.maximum(_layernorm(x, axis=-1), 0.0)
    x = x + _L0_gnn_ref(h, edge_index, edge_weight, L0_gnn_W, L0_gnn_gamma, L0_gnn_beta, 6250, 6250)
    h = jnp.maximum(_layernorm(x, axis=-1), 0.0)
    x = x + _L1_gnn_ref(h, edge_index, L1_gnn_W_msg, L1_gnn_b_msg, L1_gnn_W_upd, L1_gnn_b_upd)
    h = jnp.maximum(_layernorm(x, axis=-1), 0.0)
    x = x + _L2_gnn_ref(h, edge_index, edge_attr_64, L2_gnn_w1, L2_gnn_b1, L2_gnn_w2, L2_gnn_b2, L2_gnn_wg, L2_gnn_bg, L2_gnn_wu, L2_gnn_bu)
    h = jnp.maximum(_layernorm(x, axis=-1), 0.0)
    x = x + _L3_gnn_ref(h, node_vec1, src, dst, edge_attr_4, edge_attr_8, L3_gnn_w_lin1_s, L3_gnn_w_lin1_v, L3_gnn_fc_w1, L3_gnn_fc_w2, L3_gnn_w_lin2_s, L3_gnn_w_lin2_v)
    return x

_drawn_inputs = setup_inputs


def setup_inputs(seed=0):
    import zlib

    import numpy as np

    out = dict(_drawn_inputs(seed))
    spreads = {'L0_gnn_gamma': (1.0, 0.2), 'L0_gnn_beta': (0.0, 0.307)}
    factors = {'edge_attr_64': 8.0,
     'L1_gnn_b_upd': 4.76,
     'L2_gnn_w1': 8.0,
     'L2_gnn_b1': 33.373,
     'L2_gnn_w2': 8.0,
     'L2_gnn_b2': 48.222,
     'L2_gnn_wg': 8.0,
     'L2_gnn_bg': 29.601,
     'L2_gnn_bu': 8.0}
    for name, (base, spread) in spreads.items():
        noise = np.random.default_rng([zlib.crc32(name.encode()), seed]).standard_normal(out[name].shape)
        drawn = base * np.exp(spread * noise) if base else spread * noise
        out[name] = jnp.asarray(drawn.astype(out[name].dtype))
    for name, factor in factors.items():
        out[name] = (out[name] * factor).astype(out[name].dtype)
    return out
```

```python
from contextlib import ExitStack

import concourse.bass as bass
from concourse import mybir

ALU = mybir.AluOpType
ACT = mybir.ActivationFunctionType
F32 = mybir.dt.float32
I32 = mybir.dt.int32
AX = mybir.AxisListType

P = 128
N = 6250
E = 100000
D = 128
NB = (N + P - 1) // P
NBT = NB + 1
ROWS = (E + P - 1) // P
EPAD = ROWS * P
RING = 16
GROUP = RING // 2
CHUNKS = (ROWS + NB - 1 + P - 1) // P
ITEMS = (ROWS + NB - 1 + RING - 1) // RING * RING
META = CHUNKS * P
LEAD = 16
NOWHERE = NBT * P + 512
EP, EC = 125, E // 125
COPIES = 4
EPS = 1e-5
MUL = 32
SILU_NORM = 1.6791767923989418
L3W = 320
BIGW = NBT * 384
assert ITEMS <= META and EP * EC == E and NBT % 2 == 0


def gnn_layers(nc, x, src, dst, edge_attr_4, edge_attr_64, edge_attr_8, edge_weight,
               W0, gamma, beta, Wmsg, bmsg, Wupd, bupd, w1, b1, w2, b2, wg, bg, wu, bu,
               wl1s, wl1v, fc1, fc2, wl2s, wl2v, out):
    with ExitStack() as ctx:
        ctx.enter_context(nc.allow_non_contiguous_dma(reason="single columns and interleaved weights, once each"))

        def sb(name, shape, dt=F32):
            return ctx.enter_context(nc.sbuf_tensor(name, shape, dt))

        def sem(name):
            return ctx.enter_context(nc.semaphore(name))

        def dram(name, shape, dt=F32):
            return nc.dram_tensor(name, shape, dt, kind="Internal").ap()

        e_src, e_dst, e_w = dram("e_src", [EPAD, 1], I32), dram("e_dst", [EPAD, 1], I32), dram("e_w", [EPAD, 1])
        e_a4, e_a8, e_a64 = dram("e_a4", [EPAD, 4]), dram("e_a8", [EPAD, 8]), dram("e_a64", [EPAD, 64])
        blk_f, blk_i, bin_next = dram("blk_f", [E, 1]), dram("blk_i", [E, 1], I32), dram("bin_next", [64, 1])
        sums = [dram(f"sums{k}", [(NBT + 1) * P, 128]) for k in range(COPIES)]
        table = [None, dram("table1", [NBT * P, 128]),
                 dram("table2", [NBT * P, 256]), dram("table3", [NBT * P, 128])]

        X = sb("X", [P, NBT, D])
        big = sb("big", [P, BIGW])
        Tz = big[:, 0:NBT * 128].rearrange("p (b f) -> p b f", f=128)
        acc = [big[:, 0:NBT * 128].rearrange("p (b f) -> p b f", f=128),
               big[:, 0:NBT * 129].rearrange("p (b f) -> p b f", f=129),
               big[:, 0:NBT * 128].rearrange("p (b f) -> p b f", f=128),
               big[:, 0:NBT * L3W].rearrange("p (b f) -> p b f", f=L3W)]
        Q = big[:, NBT * 128:NBT * 384].rearrange("p (b f) -> p b f", f=256)
        src_it = sb("src_it", [P, META], I32)
        rel_it = sb("rel_it", [P, META])
        w_it = sb("w_it", [P, META])
        blk_row = sb("blk_row", [1, LEAD + META], I32)
        blk_row3 = sb("blk_row3", [1, LEAD + META], I32)
        row_row = sb("row_row", [1, LEAD + META], I32)
        G = sb("G", [P, RING, 256])
        idx = sb("idx", [P, RING], I32)
        oh = sb("oh", [P, RING, 128])
        ident, ones, iota = sb("ident", [P, P]), sb("ones", [P, P]), sb("iota", [P, P])
        tri, iota_p, icol = sb("tri", [P, P]), sb("iota_p", [P, 1]), sb("icol", [P, CHUNKS])
        bn_raw = sb("bn_raw", [P, NBT, 6])
        ln = sb("ln", [P, 5, NBT])
        MEAN, HALF, VAR, RSTD, NMR = range(5)
        deg, rdeg = sb("deg", [P, NBT]), sb("rdeg", [P, NBT])
        W0T, WmT, WuT = sb("W0T", [P, P]), sb("WmT", [P, P]), sb("WuT", [P, P])
        WPQ, We, w2s, wus = sb("WPQ", [P, 512]), sb("We", [64, 256]), sb("w2s", [P, P]), sb("wus", [P, 2, P])
        Wl1, Wl2 = sb("Wl1", [P, P]), sb("Wl2", [P, 3, P])
        fc1s, fc2s = sb("fc1s", [8, 64]), sb("fc2s", [64, 128])
        wraw = sb("wraw", [P, 3, P])
        br = sb("br", [1, 4 * P + 512])
        BR_MSG, BR_UPD, BR_B2, BR_BU, BR_Q = 0, P, 2 * P, 3 * P, 4 * P
        gam, bet, bn = sb("gam", [P, D]), sb("bet", [P, D]), sb("bn", [P, 4, D])
        a64 = sb("a64", [P, RING, 64])
        a12 = sb("a12", [P, RING, 12])
        ohT = sb("ohT", [P, 4, 128])
        aT = sb("aT", [64, 4, 128])
        pre_s = sb("pre_s", [P, 4, 256])
        sg = sb("sg", [P, 8, 256])
        sil = sb("sil", [P, 4, 128])
        silT = sb("silT", [P, 4, 128])
        msg = sb("msg", [P, 4, L3W])
        hs, src_s, sg_s, out_s = sil[:, 0:2, :], msg[:, 0:2, :], silT[:, 0:2, :], pre_s[:, 0:2, :]
        tT = sg[:, 0:4, :].rearrange("p (s q) f -> p s (q f)", s=2)
        src_b = G[:, :, 0:P].bitcast(I32)
        same = msg[:, :, 0:P]
        scaled = pre_s[:, :, 0:P]
        z_out = sg[:, :, :].rearrange("p a (c f) -> p (a c) f", c=2)
        dup, spare = sb("dup", [P, RING]), sb("spare", [P, RING])
        dup_junk, to_spare = sb("dup_junk", [P, P]), sb("to_spare", [P, META])
        cnt = sb("cnt", [P, NB + 3])
        S = sb("S", [P, NB + 3])
        Si = sb("Si", [P, 2, NB + 3], I32)
        pl = sb("pl", [P, 6, NB + 1])
        it_b, it_a = sb("it_b", [P, CHUNKS]), sb("it_a", [P, CHUNKS])
        it_ai, it_off = sb("it_ai", [P, CHUNKS], I32), sb("it_off", [P, CHUNKS])
        flag = sb("flag", [1, 1], I32)
        s_f, s_i = sb("s_f", [P, 8]), sb("s_i", [P, 4], I32)
        s_bb = sb("s_bb", [P, P])
        s_64 = sb("s_64", [P, 64])

        bank = [ctx.enter_context(nc.psum_tensor(f"bank{i}", [P, 512], F32)) for i in range(8)]

        phase_end = sem("phase_end")
        inputs_in, weights_in, const_ready, x_in = sem("inputs_in"), sem("weights_in"), sem("const_ready"), sem("x_in")
        dve_step = sem("dve_step")
        counts_ready, starts_ready, plan_ready = sem("counts_ready"), sem("starts_ready"), sem("plan_ready")
        blk_count, blocks_ready, blocks_out = sem("blk_count"), sem("blocks_ready"), sem("blocks_out")
        small_copied, a64_copied, tail_ready = sem("small_copied"), sem("a64_copied"), sem("tail_ready")
        sort_in, sort_out = [sem(f"sort_in{k}") for k in range(2)], [sem(f"sort_out{k}") for k in range(2)]
        sort_base, sort_bin = sem("sort_base"), sem("sort_bin")
        sort_rank, sort_pos, sort_go = sem("sort_rank"), sem("sort_pos"), sem("sort_go")
        meta_rows, meta_rel, meta_T, meta_out = sem("meta_rows"), sem("meta_rel"), sem("meta_T"), sem("meta_out")
        gate = sem("gate")
        gathered = [sem(f"gathered{k}") for k in range(RING)]
        attr_in = [sem(f"attr_in{k}") for k in range(RING)]
        stored = [sem(f"stored{k}") for k in range(2)]
        out_done = sem("out_done")

        def Phase(name, names):
            return {n: sem(f"{name}_{n}") for n in names.split()}

        scattered = [sem(f"scattered{k}") for k in range(COPIES)]
        zeroed, sums_in = sem("zeroed"), sem("sums_in")
        EDGE = [Phase("l0", "idx_ready oh_ready t_done ev_done row_done w_done same_ready dup_done spare_done sum_done out_ready"),
                Phase("l1", "idx_ready oh_ready agg_done acc_done"),
                Phase("l2", "idx_ready oh_ready t_done ev_done pre_done add_done sig_done sil_done "
                            "t2_done ev2_done m_done msg_done agg_done acc_done"),
                Phase("l3", "idx_ready oh_ready t_done ev_done h_done sig_done hid_done w_done "
                            "prod_done msg_done agg_done acc_done")]
        pre = Phase("pre", "stat ln_ready rstd_ready h_ready t_done tT_ready mm_done evac")
        POST = [Phase("post0", "s z a"),
                Phase("post1", "s h_ready a_ready t_done tT_ready mm_done final"),
                Phase("post2", "s a h_ready a_ready t_done tT_ready mm_done sig_done final"),
                Phase("post3", "a_ready t_done tT_ready mm_done final")]

        barrier_no = {}

        def barrier(eng):
            n = barrier_no[eng] = barrier_no.get(eng, 0) + 1
            eng.drain().then_inc(phase_end, 1)
            eng.wait_ge(phase_end, 5 * n)

        def held(eng, s, value):
            eng.wait_ge(s, value)
            eng.sem_inc(gate, 1)

        def edge_steps(eng, depth, top, body):
            top(0)
            for k in range(RING):
                body(k, k, 0, lambda lag: k >= lag)
            with eng.Fori(RING, ITEMS, RING) as turn:
                top(turn)
                for k in range(RING):
                    body(turn + k, k, turn, lambda lag: True)
            top(ITEMS)
            for k in range(depth):
                body(ITEMS + k, k, ITEMS, lambda lag: k < lag)

        def dma_value(per_item, before, turn, k, lag):
            uses = (turn if per_item == 16 else turn * (per_item // 16))
            return uses + before + per_item * ((k - lag) // RING + 1)

        G_USES = 16 * (ITEMS // RING)
        A_BEFORE = {0: 0, 2: 16 * (ITEMS // RING), 3: 32 * (ITEMS // RING)}

        def block_steps(eng, depth, body):
            for b in range(4):
                body(b, b % 2, lambda lag: b >= lag)
            with eng.Fori(2, NBT // 2) as pair:
                body(pair * 2, 0, lambda lag: True)
                body(pair * 2 + 1, 1, lambda lag: True)
            for b in range(NBT, NBT + depth):
                body(b, b % 2, lambda lag: b - NBT < lag)

        def at(a, b):
            return a[:, bass.ds(b, 1), :].rearrange("p o f -> p (o f)")

        raw_dst = big[0:EP, 0:2 * EC].bitcast(I32)
        blk_floats = big[0:EP, 2 * EC:3 * EC + 1]
        blk_next = big[0:EP, 6 * EC:7 * EC + 1].bitcast(I32)
        blk_ids = blk_next[:, 0:EC]

        row = lambda v: v.rearrange("(a n) -> a n", a=1)
        loads = [(wraw[:, 0, :], W0), (wraw[:, 1, :], Wmsg), (wraw[:, 2, :], Wupd),
                 (WPQ[:, 0:128], w1[0:128, :]), (WPQ[:, 128:256], wg[0:128, :]),
                 (WPQ[:, 256:384], w1[128:256, :]), (WPQ[:, 384:512], wg[128:256, :]),
                 (We[:, 0:128], w1[256:320, :]), (We[:, 128:256], wg[256:320, :]),
                 (w2s[:], w2), (wus[:, 0, :], wu[0:128, :]), (wus[:, 1, :], wu[128:256, :]),
                 (fc1s[:], fc1), (fc2s[:], fc2),
                 (br[:, BR_MSG:BR_MSG + P], row(bmsg)), (br[:, BR_UPD:BR_UPD + P], row(bupd)),
                 (br[:, BR_B2:BR_B2 + P], row(b2)), (br[:, BR_BU:BR_BU + P], row(bu)),
                 (br[:, BR_Q + 256:BR_Q + 384], row(b1)), (br[:, BR_Q + 384:BR_Q + 512], row(bg)),
                 (gam[:], gamma.partition_broadcast(P)), (bet[:], beta.partition_broadcast(P)),
                 (Wl1[0:32, 0:32], wl1s),
                 (Wl2[0:32, 0, 0:32], wl2s[0:32, :]), (Wl2[32:64, 1, 0:32], wl2s[32:64, :]),
                 (Wl2[96:128, 1, 0:32], wl2s[32:64, :]), (Wl2[32:64, 2, 0:32], wl2s[32:64, :])]
        for i in range(3):
            loads += [(Wl1[32 + i:P:3, 32 + 32 * i:64 + 32 * i], wl1v),
                      (Wl2[32 + 32 * i:64 + 32 * i, 0, 32 + i::3], wl2v[32:64, :]),
                      (Wl2[64 * (i % 2):64 * (i % 2) + 32, 1 + i // 2, 32 + i::3], wl2v[0:32, :])]
        N_LOADS = 2 + len(loads)

        block = ctx.enter_context(nc.Block())

        @block.sync
        def _(sp):
            sp.dma_start(raw_dst[:, 0:EC], dst.rearrange("(p c) -> p c", p=EP)).then_inc(inputs_in, 16)
            sp.dma_start(raw_dst[0:EP - 1, EC:EC + 1],
                         dst.rearrange("(p c) -> p c", p=EP)[1:EP, 0:1]).then_inc(inputs_in, 16)
            sp.wait_ge(x_in, 1)
            sp.dma_start(X[:, 0:NB - 1, :], x[0:(NB - 1) * P, :].rearrange("(b p) d -> p b d", p=P)).then_inc(weights_in, 16)
            sp.dma_start(X[0:N - (NB - 1) * P, NB - 1, :], x[(NB - 1) * P:N, :]).then_inc(weights_in, 16)
            for to, of in loads:
                sp.dma_start(to, of).then_inc(weights_in, 16)
            sp.wait_ge(blocks_ready, 1)
            sp.dma_start(blk_i[:, :].rearrange("(p c) o -> p (c o)", p=EP), blk_ids).then_inc(blocks_out, 16)
            sp.dma_start(blk_f[:, :].rearrange("(p c) o -> p (c o)", p=EP), blk_floats[:, 0:EC]).then_inc(blocks_out, 16)
            sp.wait_ge(blocks_ready, 2)
            sp.dma_start(bin_next, s_f[0:64, 5:6]).then_inc(blocks_out, 16)
            barrier(sp)

            def store_table(layer, before):
                u, wid = NBT * layer, table[layer].shape[1]

                def body(b, s, live):
                    sp.wait_ge(pre["evac"], b + (1 + u))
                    sp.dma_start(table[layer][bass.ds(b * P, P), :], out_s[:, s, 0:wid]).then_inc(stored[s], 16)
                block_steps(sp, 0, body)
                for s in range(2):
                    sp.wait_ge(stored[s], before + 16 * (NBT // 2))
                barrier(sp)

            def load_attributes(layer):
                ph = EDGE[layer]
                freed = ph["dup_done"] if layer == 0 else ph["t_done"] if layer == 2 else ph["msg_done"]
                regs = [sp.alloc_register(f"row{layer}_{k}") for k in range(RING)]

                def top(turn):
                    sp.load(regs, row_row[0:1, bass.ds(turn + LEAD, RING)])

                def load(k, turn):
                    r = sp.snap(regs[k], min_val=0, max_val=ROWS - 1)
                    if layer == 0:
                        sp.dma_start(src_b[:, k, :], e_src[bass.ds(r * P, P), :].rearrange("e o -> (o e)").partition_broadcast(P)
                                     ).then_inc(attr_in[k], 16)
                    elif layer == 2:
                        sp.dma_start(a64[:, k, :], e_a64[bass.ds(r * P, P), :]).then_inc(attr_in[k], 16)
                    else:
                        sp.dma_start(a12[:, k, 0:8], e_a8[bass.ds(r * P, P), :]).then_inc(attr_in[k], 16)
                        sp.dma_start(a12[:, k, 8:12], e_a4[bass.ds(r * P, P), :]).then_inc(attr_in[k], 16)

                top(0)
                for k in range(RING):
                    load(k, 0)
                with sp.Fori(RING, ITEMS, RING) as turn:
                    top(turn)
                    for k in range(RING):
                        held(sp, freed, turn + (k - RING + 1))
                        load(k, turn)

            for layer in range(4):
                if layer:
                    store_table(layer, 16 * (NBT // 2) * (layer - 1))
                else:
                    barrier(sp)
                if layer == 2:
                    sp.wait_ge(a64_copied, 48)
                if layer != 1:
                    load_attributes(layer)
                barrier(sp)
                if layer == 3:
                    barrier(sp)
                    sp.dma_start(out[0:(NB - 1) * P, :].rearrange("(b p) d -> p b d", p=P), X[:, 0:NB - 1, :]).then_inc(out_done, 16)
                    sp.dma_start(out[(NB - 1) * P:N, :], X[0:N - (NB - 1) * P, NB - 1, :]).then_inc(out_done, 16)
                    sp.wait_ge(out_done, 32)
                elif layer == 0:
                    for k in range(COPIES):
                        if k == COPIES - 1:
                            sp.wait_ge(POST[0]["s"], 1)
                        q = k if k < COPIES - 1 else 1
                        sp.dma_start(big[:, q * NBT * 128:(q + 1) * NBT * 128].rearrange("p (b f) -> p b f", f=128),
                                     sums[k][0:NBT * P, :].rearrange("(b p) d -> p b d", p=P)).then_inc(sums_in, 16)
                        if k >= COPIES - 2:
                            sp.wait_ge(sums_in, 16 * (k + 1))
                    barrier(sp)
                else:
                    barrier(sp)

        @block.gpsimd
        def _(pool):
            g = nc.gpsimd
            g.memset(X[:, NB - 1:NBT, :], 0.0)
            g.memset(Wl1[:], 0.0)
            g.memset(Wl2[:], 0.0)
            g.memset(br[:, BR_Q:BR_Q + 256], 0.0)
            g.memset(ones[:], 1.0)
            g.memset(cnt[:], 0.0)
            g.memset(G[:, :, 128:129], 1.0)
            g.memset(blk_row[:], 0)
            g.memset(blk_row3[:], 0)
            g.memset(row_row[:], 0)
            pool.drain().then_inc(x_in, 1)
            g.memset(ident[:], 0.0).then_inc(const_ready, 1)
            g.memset(tri[:], 1.0).then_inc(const_ready, 1)
            g.memset(s_64[:], 0.0)
            g.memset(s_f[:, 0:1], 0.0)
            g.memset(s_i[:, 0:1], 0)
            g.memset(s_i[:, 1:2], NOWHERE).then_inc(tail_ready, 1)
            g.iota(iota[:], [[1, P]], base=0, channel_multiplier=0, allow_small_or_imprecise_dtypes=True)
            g.iota(iota_p[:], [[0, 1]], base=0, channel_multiplier=1, allow_small_or_imprecise_dtypes=True)
            g.iota(icol[:], [[P, CHUNKS]], base=0, channel_multiplier=1, allow_small_or_imprecise_dtypes=True)
            pool.wait_ge(const_ready, 2)
            g.affine_select(out=ident[:], in_=ident[:], compare_op=ALU.not_equal, fill=1.0, base=0,
                            pattern=[[-1, P]], channel_multiplier=1)
            g.affine_select(out=tri[:], in_=tri[:], compare_op=ALU.is_gt, fill=0.0, base=0,
                            pattern=[[-1, P]], channel_multiplier=1).then_inc(const_ready, 1)

            T0, TN = E, EPAD - E
            pool.wait_ge(tail_ready, 1)

            def tails():
                for to, of in ((e_src, s_i[0:TN, 0:1]), (e_dst, s_i[0:TN, 1:2]), (e_w, s_f[0:TN, 0:1]),
                               (e_a4, s_64[0:TN, 0:4]), (e_a8, s_64[0:TN, 0:8]), (e_a64, s_64[0:TN, 0:64])):
                    pool.dma_start(to[T0:EPAD, :], of).then_inc(small_copied, 16)
            tails()
            pool.wait_ge(small_copied, 6 * 16)

            pool.wait_ge(plan_ready, 1)
            falls = pool.value_load(flag[0:1, 0:1], min_val=0, max_val=E)
            flat = lambda a, c: a.rearrange("(q c) o -> q (c o)", c=c)
            with pool.If(falls == 0):
                for to, of in ((e_src, src), (e_dst, dst), (e_w, edge_weight)):
                    pool.dma_start(flat(to[0:E, :], EC), of.rearrange("(q c) -> q c", c=EC)).then_inc(small_copied, 16)
                for to, of, q in ((e_a4, edge_attr_4, 160), (e_a8, edge_attr_8, 160), (e_a64, edge_attr_64, 3200)):
                    even = lambda a: a.rearrange("e k -> (e k)").rearrange("(q c) -> q c", q=q)
                    pool.dma_start(even(to[0:E, :]), even(of)).then_inc(a64_copied, 16)
                pool.wait_ge(small_copied, 9 * 16)
            with pool.Else():
                pool.wait_ge(blocks_out, 48)

                def tile(t, e0, n, first):
                    sl = slice(e0, e0 + n) if isinstance(e0, int) else bass.ds(e0, n)
                    if not first:
                        held(pool, sort_pos, t)
                        for k in range(2):
                            held(pool, sort_out[k], t * 48)
                        held(pool, sort_bin, t * 16)
                    pool.dma_start(s_bb[:, 0:n], blk_f[sl, :].rearrange("e o -> o e").partition_broadcast(P)).then_inc(sort_in[0], 16)
                    for q, (to, of) in enumerate(((s_f[0:n, 1:2], blk_f[sl, :]), (s_i[0:n, 2:3], blk_i[sl, :]),
                                   (s_i[0:n, 0:1], src[sl].rearrange("(e o) -> e o", o=1)),
                                   (s_i[0:n, 1:2], dst[sl].rearrange("(e o) -> e o", o=1)),
                                   (s_f[0:n, 0:1], edge_weight[sl].rearrange("(e o) -> e o", o=1)),
                                   (a12[0:n, 0, 0:4], edge_attr_4[sl, :]), (a12[0:n, 1, 0:8], edge_attr_8[sl, :]),
                                   (s_64[0:n, :], edge_attr_64[sl, :]))):
                        pool.dma_start(to, of).then_inc(sort_in[q // 4], 16)
                    held(pool, sort_in[0], t * 80 + 80)
                    held(pool, sort_in[1], t * 64 + 64)
                    pool.indirect_dma_start(s_f[0:n, 2:3], None, bin_next,
                                            bass.IndirectOffsetOnAxis(ap=s_i[0:n, 2:3], axis=0)).then_inc(sort_base, 16)
                    held(pool, sort_rank, t + 1)
                    pool.dma_start(bin_next, s_f[0:64, 5:6]).then_inc(sort_bin, 16)
                    at = bass.IndirectOffsetOnAxis(ap=s_i[0:n, 3:4], axis=0)
                    for q, (to, of) in enumerate(((e_src, s_i[0:n, 0:1]), (e_dst, s_i[0:n, 1:2]), (e_w, s_f[0:n, 0:1]),
                                                  (e_a4, a12[0:n, 0, 0:4]), (e_a8, a12[0:n, 1, 0:8]), (e_a64, s_64[0:n, :]))):
                        pool.indirect_dma_start(to, at, of, None).then_inc(sort_out[q // 3], 16)
                full = E // P
                tile(0, 0, P, True)
                with pool.Fori(1, full) as t:
                    tile(t, t * P, P, False)
                tile(full, full * P, E - full * P, False)
                for k in range(2):
                    pool.wait_ge(sort_out[k], (full + 1) * 48)
                g.memset(s_64[:], 0.0).then_inc(tail_ready, 1)
                pool.wait_ge(tail_ready, 2)
                for _ in range(3):
                    pool.dma_start(blk_f[0:P, :], s_64[:, 0:1]).then_inc(a64_copied, 16)
                    pool.wait_ge(a64_copied, 16 * (_ + 1))
            pool.nop()
            pool.wait_ge(blocks_out, 48)

            rows128 = lambda a: a.rearrange("(r e) o -> r (e o)", e=P)
            m_i = big[:, 0:2 * META].bitcast(I32)
            m_w = big[:, 2 * META:3 * META]
            for c in range(CHUNKS):
                at = bass.IndirectOffsetOnAxis(ap=it_ai[:, c:c + 1], axis=0)
                pool.indirect_dma_start(m_i[:, c * P:(c + 1) * P], None, rows128(e_src), at).then_inc(meta_rows, 16)
                pool.indirect_dma_start(m_i[:, META + c * P:META + (c + 1) * P], None, rows128(e_dst), at).then_inc(meta_rows, 16)
                pool.indirect_dma_start(m_w[:, c * P:(c + 1) * P], None, rows128(e_w), at).then_inc(meta_rows, 16)
            barrier(pool)

            g.memset(big[:, NBT * P:(2 * NBT + 1) * P], 0.0).then_inc(zeroed, 1)
            pool.wait_ge(zeroed, 1)
            for k in range(COPIES):
                pool.dma_start(sums[k].rearrange("(b p) d -> p b d", p=P),
                               big[:, NBT * P:(2 * NBT + 1) * P].rearrange("p (b f) -> p b f", f=128)).then_inc(scattered[k], 16)
                pool.wait_ge(scattered[k], 16)
            barrier(pool)
            ph = EDGE[0]

            def scatter(turn, k, i, uses):
                if k % GROUP == 0:
                    held(pool, ph["idx_ready"], uses[0])
                held(pool, ph["out_ready"], i + 1)
                held(pool, scattered[k % COPIES], uses[1])
                pool.indirect_dma_start(sums[k % COPIES], bass.IndirectOffsetOnAxis(ap=idx[:, k:k + 1], axis=0),
                                        z_out[:, k, :], None, compute_op=ALU.add).then_inc(scattered[k % COPIES], 16)
            with pool.Fori(0, ITEMS // RING) as turn:
                for k in range(RING):
                    scatter(turn, k, turn * RING + k,
                            (turn * 2 + k // GROUP + 1, turn * (16 * RING // COPIES) + 16 * (k // COPIES + 1)))
            for k in range(COPIES):
                pool.wait_ge(scattered[k], 16 * (ITEMS // COPIES + 1))
            barrier(pool)
            barrier(pool)

            for layer in range(1, 4):
                wid = acc[layer].shape[2]
                g.memset(big[:, 0:NBT * wid], 0.0)
                barrier(pool)
                ph, tab, wid = EDGE[layer], table[layer], table[layer].shape[1]
                with pool.Fori(0, ITEMS // RING) as turn:
                    for h in range(2):
                        held(pool, ph["idx_ready"], turn * 2 + h + 1)
                        for k in range(h * GROUP, (h + 1) * GROUP):
                            pool.indirect_dma_start(G[:, k, 0:wid], None, tab,
                                                    bass.IndirectOffsetOnAxis(ap=idx[:, k:k + 1], axis=0)).then_inc(gathered[k], 16)
                barrier(pool)
                barrier(pool)

        @block.tensor
        def _(pe):
            t = nc.tensor
            pe.wait_ge(const_ready, 3)
            pe.wait_ge(counts_ready, 1)
            t.matmul(bank[0][:, 0:NB + 3], ones[0:EP, :], cnt[0:EP, :], start=True, stop=True).then_inc(starts_ready, 1)
            pe.wait_ge(weights_in, 16 * N_LOADS)
            for k in range(3):
                mm = t.transpose(bank[7][:, k * P:(k + 1) * P], wraw[:, k, :], ident[:])
            mm.then_inc(meta_T, 1)
            m_f = big[:, 3 * META:6 * META]
            pe.wait_ge(meta_rel, 1)
            for q in range(3 * CHUNKS):
                b = q % 6
                if q >= 6:
                    pe.wait_ge(meta_out, q - 5)
                t.transpose(bank[1 + b][:, 0:P], m_f[:, q * P:(q + 1) * P], ident[:]).then_inc(meta_T, 1)
            for c in range(CHUNKS):
                pe.wait_ge(meta_out, 3 * CHUNKS)
                t.transpose(bank[0][0:1, (c % 4) * P:(c % 4 + 1) * P] if c < 4 else bank[1][0:1, (c % 4) * P:(c % 4 + 1) * P],
                            it_b[:, c:c + 1], ident[:])
                mm = t.transpose(bank[2][0:1, (c % 4) * P:(c % 4 + 1) * P] if c < 4 else bank[3][0:1, (c % 4) * P:(c % 4 + 1) * P],
                                 it_a[:, c:c + 1], ident[:])
            mm.then_inc(meta_T, 1)
            barrier(pe)

            def node_tables(layer):
                u = NBT * layer
                Wt = [W0T, WmT, WPQ, Wl1][layer][:]
                n = Wt.shape[1]
                bias = {1: br[:, BR_MSG:BR_MSG + P], 2: br[:, BR_Q:BR_Q + 512]}.get(layer)

                def body(b, s, live):
                    if live(0):
                        pe.wait_ge(pre["h_ready"], b + (1 + u))
                        if live(2):
                            pe.wait_ge(pre["tT_ready"], b + (u - 1))
                        t.transpose(bank[s][:, 0:P], hs[:, s, :], ident[:]).then_inc(pre["t_done"], 1)
                    if live(1):
                        o = 1 - s
                        if live(1 + 2):
                            pe.wait_ge(pre["evac"], b + (u - 2))
                        pe.wait_ge(pre["tT_ready"], b + u)
                        mm = t.matmul(bank[2 + o][:, 0:n], tT[:, o, 0:P], Wt, start=True, stop=bias is None)
                        if bias is not None:
                            mm = t.matmul(bank[2 + o][:, 0:n], ones[0:1, :], bias, start=False, stop=True)
                        mm.then_inc(pre["mm_done"], 1)
                block_steps(pe, 1, body)
                barrier(pe)

            def aggregate(layer):
                ph, wid = EDGE[layer], acc[layer].shape[2]

                def body(n, k, turn, live):
                    if live(3):
                        s = (k - 3) % RING
                        pe.wait_ge(gathered[s], dma_value(16, (layer - 1) * G_USES, turn, k, 3))
                        if live(3 + 4):
                            pe.wait_ge(ph["acc_done"], n - 3 - 3)
                        pe.wait_ge(ph["oh_ready"], n - 3 + 1)
                        t.matmul(bank[s % 4][:, 0:wid], oh[:, s, :], G[:, s, 0:wid], start=True, stop=True).then_inc(ph["agg_done"], 1)
                edge_steps(pe, 3, lambda turn: None, body)
                barrier(pe)

            def edges0():
                ph = EDGE[0]
                regs = [pe.alloc_register(f"zblk{k}") for k in range(RING)]

                def top(turn):
                    pe.load(regs, blk_row3[0:1, bass.ds(turn + LEAD, RING)])

                def body(n, k, turn, live):
                    if live(1):
                        s = (k - 1) % RING
                        if live(1 + 2):
                            pe.wait_ge(ph["ev_done"], n - 1 - 1)
                        pe.wait_ge(ph["oh_ready"], n - 1 + 1)
                        t.transpose(bank[s % 2][:, 0:P], oh[:, s, :], ident[:]).then_inc(ph["t_done"], 1)
                    if live(3):
                        s = (k - 3) % RING
                        if live(3 + 2):
                            pe.wait_ge(ph["w_done"], n - 3 - 1)
                        pe.wait_ge(ph["ev_done"], n - 3 + 1)
                        b = pe.snap(regs[k], min_val=0, max_val=NB)
                        t.matmul(bank[2 + s % 2][:, 0:P], ohT[:, s % 4, :], at(Tz, b), start=True, stop=True).then_inc(ph["row_done"], 1)
                    if live(5):
                        s = (k - 5) % RING
                        if live(5 + 2):
                            pe.wait_ge(ph["out_ready"], n - 5 - 1)
                        pe.wait_ge(ph["same_ready"], n - 5 + 1)
                        pe.wait_ge(ph["w_done"], n - 5 + 1)
                        t.matmul(bank[4 + s % 2][:, 0:P], same[:, s % 4, :], scaled[:, s % 4, :], start=True, stop=True).then_inc(ph["sum_done"], 1)
                edge_steps(pe, 5, top, body)
                barrier(pe)

            def edges2():
                ph = EDGE[2]
                regs = [pe.alloc_register(f"qblk{k}") for k in range(RING)]

                def top(turn):
                    pe.load(regs, blk_row3[0:1, bass.ds(turn + LEAD, RING)])

                def body(n, k, turn, live):
                    if live(1):
                        s = (k - 1) % RING
                        if live(1 + 2):
                            pe.wait_ge(ph["ev_done"], n - 1 - 1)
                        pe.wait_ge(attr_in[s], dma_value(16, A_BEFORE[2], turn, k, 1))
                        pe.wait_ge(ph["oh_ready"], n - 1 + 1)
                        t.transpose(bank[s % 2][:, 0:P], oh[:, s, :], ident[:])
                        t.transpose(bank[s % 2][0:64, P:2 * P], a64[:, s, :], ident[:]).then_inc(ph["t_done"], 1)
                    if live(3):
                        s = (k - 3) % RING
                        if live(3 + 2):
                            pe.wait_ge(ph["add_done"], n - 3 - 1)
                        pe.wait_ge(ph["ev_done"], n - 3 + 1)
                        b = pe.snap(regs[k], min_val=0, max_val=NB)
                        t.matmul(bank[2 + s % 2][:, 0:256], ohT[:, s % 4, :],
                                 Q[:, bass.ds(b, 1), :].rearrange("p o f -> p (o f)"), start=True, stop=False)
                        t.matmul(bank[2 + s % 2][:, 0:256], aT[:, s % 4, :], We[:], start=False, stop=True).then_inc(ph["pre_done"], 1)
                    if live(7):
                        s = (k - 7) % RING
                        if live(7 + 1):
                            pe.wait_ge(ph["ev2_done"], n - 7)
                        pe.wait_ge(ph["sil_done"], n - 7 + 1)
                        t.transpose(bank[4][:, 0:P], sil[:, s % 4, :], ident[:]).then_inc(ph["t2_done"], 1)
                    if live(8):
                        s = (k - 8) % RING
                        if live(8 + 1):
                            pe.wait_ge(ph["msg_done"], n - 8)
                        pe.wait_ge(ph["ev2_done"], n - 8 + 1)
                        t.matmul(bank[5][:, 0:P], silT[:, s % 4, :], w2s[:], start=True, stop=False)
                        t.matmul(bank[5][:, 0:P], ones[0:1, :], br[:, BR_B2:BR_B2 + P], start=False, stop=True).then_inc(ph["m_done"], 1)
                    if live(11):
                        s = (k - 11) % RING
                        if live(11 + 2):
                            pe.wait_ge(ph["acc_done"], n - 11 - 1)
                        pe.wait_ge(ph["msg_done"], n - 11 + 1)
                        t.matmul(bank[6 + s % 2][:, 0:P], oh[:, s, :], msg[:, s % 4, 0:P], start=True, stop=True).then_inc(ph["agg_done"], 1)
                edge_steps(pe, 11, top, body)
                barrier(pe)

            def edges3():
                ph = EDGE[3]

                def body(n, k, turn, live):
                    if live(1):
                        s = (k - 1) % RING
                        if live(1 + 2):
                            pe.wait_ge(ph["ev_done"], n - 1 - 1)
                        pe.wait_ge(attr_in[s], dma_value(32, A_BEFORE[3], turn, k, 1))
                        t.transpose(bank[(0, 4)[s % 2]][0:8, 0:P], a12[:, s, 0:8], ident[:]).then_inc(ph["t_done"], 1)
                    if live(3):
                        s = (k - 3) % RING
                        if live(3 + 2):
                            pe.wait_ge(ph["hid_done"], n - 3 - 1)
                        pe.wait_ge(ph["ev_done"], n - 3 + 1)
                        t.matmul(bank[(1, 5)[s % 2]][0:64, 0:P], fc1s[:], aT[0:8, s % 4, :], start=True, stop=True).then_inc(ph["h_done"], 1)
                    if live(5):
                        s = (k - 5) % RING
                        if live(5 + 2):
                            pe.wait_ge(ph["prod_done"], n - 5 - 1)
                        pe.wait_ge(ph["hid_done"], n - 5 + 1)
                        t.matmul(bank[2 + s % 2][:, 0:P], silT[0:64, s % 4, :], fc2s[:], start=True, stop=True).then_inc(ph["w_done"], 1)
                    if live(8):
                        s = (k - 8) % RING
                        if live(8 + 2):
                            pe.wait_ge(ph["acc_done"], n - 8 - 1)
                        pe.wait_ge(ph["oh_ready"], n - 8 + 1)
                        pe.wait_ge(ph["msg_done"], n - 8 + 1)
                        t.matmul(bank[6 + s % 2][:, 0:L3W], oh[:, s, :], msg[:, s % 4, :], start=True, stop=True).then_inc(ph["agg_done"], 1)
                edge_steps(pe, 8, lambda turn: None, body)
                barrier(pe)

            def node_updates(layer):
                ph = POST[layer]
                parts = {1: [(src_s, 0, P, WuT[:])],
                         2: [(hs, 0, P, wus[:, 0, :]), (src_s, 0, P, wus[:, 1, :])],
                         3: [(src_s, 0, P, Wl2[:, 0, :]), (src_s, P, P, Wl2[:, 1, :]), (src_s, 2 * P, 64, Wl2[0:64, 2, :])]}[layer]
                bias = {1: br[:, BR_UPD:BR_UPD + P], 2: br[:, BR_BU:BR_BU + P]}.get(layer)

                def body(b, s, live):
                    if live(0):
                        if layer == 2:
                            pe.wait_ge(ph["h_ready"], b + 1)
                        pe.wait_ge(ph["a_ready"], b + 1)
                        if live(2):
                            pe.wait_ge(ph["tT_ready"], b - 1)
                        for q, (of, c, w, _) in enumerate(parts):
                            mm = t.transpose(bank[s][0:w, q * P:(q + 1) * P], of[:, s, c:c + w], ident[:])
                        mm.then_inc(ph["t_done"], 1)
                    if live(1):
                        o = 1 - s
                        if live(1 + 2):
                            pe.wait_ge(ph["final"], b - 2)
                        pe.wait_ge(ph["tT_ready"], b)
                        for q, (_, c, w, weights) in enumerate(parts):
                            mm = t.matmul(bank[2 + o][:, 0:P], tT[0:w, o, q * P:(q + 1) * P], weights,
                                          start=(q == 0), stop=(q == len(parts) - 1 and bias is None))
                        if bias is not None:
                            mm = t.matmul(bank[2 + o][:, 0:P], ones[0:1, :], bias, start=False, stop=True)
                        mm.then_inc(ph["mm_done"], 1)
                block_steps(pe, 1, body)
                barrier(pe)

            def batch_sums():
                for which, of in enumerate((acc[0], big[:, NBT * 128:2 * NBT * 128].rearrange("p (b f) -> p b f", f=128))):
                    pe.wait_ge(POST[0]["s"], 2 + which)
                    for b in range(NB):
                        rows = P if b < NB - 1 else N - (NB - 1) * P
                        mm = t.matmul(bank[which][:, 0:P], ones[0:rows, :], of[0:rows, b, :], start=(b == 0), stop=(b == NB - 1))
                    mm.then_inc(POST[0]["z"], 1)
                barrier(pe)

            for layer in range(4):
                node_tables(layer)
                [edges0, lambda: aggregate(1), edges2, edges3][layer]()
                if layer == 0:
                    batch_sums()
                else:
                    node_updates(layer)

        @block.scalar
        def _(act):
            a = nc.scalar
            barrier(act)

            def normed(ph, b, s, reused, release, before=0):
                if reused:
                    act.wait_ge(release, b + (before - 1))
                a.activation(hs[:, s, :], at(X, b), ACT.Relu, scale=ln[:, RSTD, bass.ds(b, 1)],
                             bias=ln[:, NMR, bass.ds(b, 1)]).then_inc(ph["h_ready"], 1)

            def node_tables(layer):
                u = NBT * layer
                act.wait_ge(pre["ln_ready"], 2 * layer + 1)
                a.activation(ln[:, RSTD, :], ln[:, VAR, :], ACT.Sqrt).then_inc(pre["rstd_ready"], 1)
                act.wait_ge(pre["ln_ready"], 2 * layer + 2)
                wid = table[layer].shape[1] if layer else P
                func = ACT.Relu if layer == 1 else ACT.Copy

                def body(b, s, live):
                    if live(0):
                        normed(pre, b, s, live(2), pre["t_done"], u)
                    if live(2):
                        act.wait_ge(pre["mm_done"], b + (u - 1))
                        if layer == 0:
                            a.activation(at(Tz, b - 2), bank[2 + s][:, 0:P], ACT.Copy).then_inc(pre["evac"], 1)
                            return
                        if live(2 + 2) or layer > 1:
                            act.wait_ge(stored[s], 16 * (NBT // 2) * (layer - 1) + (b - 2 - s) * 8)
                        if layer == 2:
                            a.activation(at(Q, b - 2), bank[2 + s][:, 256:512], ACT.Copy)
                        a.activation(out_s[:, s, 0:wid], bank[2 + s][:, 0:wid], func).then_inc(pre["evac"], 1)
                block_steps(act, 2, body)
                barrier(act)

            def copy_indices(ph, start, half):
                a.activation(idx[:, half * GROUP:(half + 1) * GROUP], src_it[:, bass.ds(start, GROUP)], ACT.Copy).then_inc(ph["idx_ready"], 1)

            def aggregate(layer):
                ph = EDGE[layer]
                copy_indices(ph, 0, 0)
                copy_indices(ph, GROUP, 1)
                with act.Fori(RING, ITEMS, RING) as turn:
                    for h in range(2):
                        act.wait_ge(ph["agg_done"], turn + (h * GROUP - GROUP))
                        copy_indices(ph, turn + h * GROUP, h)
                barrier(act)

            def edges0():
                ph = EDGE[0]

                def body(n, k, turn, live):
                    if live(2):
                        s = (k - 2) % RING
                        act.wait_ge(ph["t_done"], n - 2 + 1)
                        if live(2 + 4):
                            act.wait_ge(ph["row_done"], n - 2 - 3)
                        a.activation(ohT[:, s % 4, :], bank[s % 2][:, 0:P], ACT.Copy).then_inc(ph["ev_done"], 1)
                    if live(4):
                        s = (k - 4) % RING
                        act.wait_ge(ph["row_done"], n - 4 + 1)
                        if live(4 + 4):
                            act.wait_ge(ph["sum_done"], n - 4 - 3)
                        a.activation(scaled[:, s % 4, :], bank[2 + s % 2][:, 0:P], ACT.Copy,
                                     scale=w_it[:, bass.ds(n - 4, 1)]).then_inc(ph["w_done"], 1)
                edge_steps(act, 4, lambda turn: None, body)
                barrier(act)

            def edges2():
                ph = EDGE[2]
                copy_indices(ph, 0, 0)
                copy_indices(ph, GROUP, 1)

                def body(n, k, turn, live):
                    if live(2):
                        s = (k - 2) % RING
                        act.wait_ge(ph["t_done"], n - 2 + 1)
                        if live(2 + 4):
                            act.wait_ge(ph["pre_done"], n - 2 - 3)
                        a.activation(ohT[:, s % 4, :], bank[s % 2][:, 0:P], ACT.Copy)
                        a.activation(aT[:, s % 4, :], bank[s % 2][0:64, P:2 * P], ACT.Copy).then_inc(ph["ev_done"], 1)
                    if live(5):
                        s = (k - 5) % RING
                        act.wait_ge(ph["add_done"], n - 5 + 1)
                        if live(5 + 8):
                            act.wait_ge(ph["msg_done"], n - 5 - 7)
                        a.activation(sg[:, s % 8, :], pre_s[:, s % 4, :], ACT.Sigmoid).then_inc(ph["sig_done"], 1)
                    if live(7):
                        s = (k - 7) % RING
                        act.wait_ge(ph["t2_done"], n - 7 + 1)
                        if live(7 + 4):
                            act.wait_ge(ph["m_done"], n - 7 - 3)
                        a.activation(silT[:, s % 4, :], bank[4][:, 0:P], ACT.Copy).then_inc(ph["ev2_done"], 1)
                    if k % GROUP == GROUP - 1 and (not isinstance(n, int) or 15 <= n < ITEMS - 1):
                        act.wait_ge(ph["add_done"], n + 1 - GROUP)
                        copy_indices(ph, n + 1, (k + 1) // GROUP % 2)
                edge_steps(act, 7, lambda turn: None, body)
                barrier(act)

            def edges3():
                ph = EDGE[3]
                copy_indices(ph, 0, 0)
                copy_indices(ph, GROUP, 1)

                def body(n, k, turn, live):
                    if live(2):
                        s = (k - 2) % RING
                        act.wait_ge(ph["t_done"], n - 2 + 1)
                        if live(2 + 4):
                            act.wait_ge(ph["h_done"], n - 2 - 3)
                        a.activation(aT[0:8, s % 4, :], bank[(0, 4)[s % 2]][0:8, 0:P], ACT.Copy).then_inc(ph["ev_done"], 1)
                    if live(3):
                        s = (k - 3) % RING
                        act.wait_ge(ph["h_done"], n - 3 + 1)
                        if live(3 + 4):
                            act.wait_ge(ph["hid_done"], n - 3 - 3)
                        a.activation(sg[0:64, s % 4, 0:P], bank[(1, 5)[s % 2]][0:64, 0:P], ACT.Sigmoid).then_inc(ph["sig_done"], 1)
                    if live(7):
                        s = (k - 7) % RING
                        act.wait_ge(ph["prod_done"], n - 7 + 1)
                        if live(7 + 4):
                            act.wait_ge(ph["agg_done"], n - 7 - 3)
                        pr = pre_s[:, s % 4, :]
                        a.activation(msg[:, s % 4, 0:P], pr[:, 0:P], ACT.Copy, scale=a12[:, s, 8:9])
                        for i in range(3):
                            pair = pr[:, P:2 * P].rearrange("p (c f) -> p c f", f=MUL)[:, 0:i + 2:i + 1, :]
                            to = msg[:, s % 4, P + 64 * i:P + 64 * i + 64].rearrange("p (c f) -> p c f", f=MUL)
                            last = a.activation(to, pair, ACT.Copy, scale=a12[:, s, 9 + i:10 + i])
                        last.then_inc(ph["msg_done"], 1)
                    if k % GROUP == GROUP - 1 and (not isinstance(n, int) or 15 <= n < ITEMS - 1):
                        act.wait_ge(ph["prod_done"], n + 1 - GROUP)
                        copy_indices(ph, n + 1, (k + 1) // GROUP % 2)
                edge_steps(act, 7, lambda turn: None, body)
                barrier(act)

            def node_updates(layer):
                ph, wid = POST[layer], {1: P, 2: P, 3: L3W}[layer]
                if layer == 2:
                    act.wait_ge(ph["a"], 1)

                def body(b, s, live):
                    if live(0):
                        if layer < 3:
                            normed(ph, b, s, live(2), ph["final"] if layer == 1 else ph["t_done"])
                        if live(2):
                            act.wait_ge(ph["t_done"], b - 1)
                        of = acc[layer][:, bass.ds(b, 1), 0:wid].rearrange("p o f -> p (o f)")
                        scale = rdeg[:, bass.ds(b, 1)] if layer == 2 else 1.0
                        a.activation(src_s[:, s, 0:wid], of, ACT.Copy, scale=scale).then_inc(ph["a_ready"], 1)
                    if live(1) and layer == 2:
                        act.wait_ge(ph["mm_done"], b)
                        if live(1 + 2):
                            act.wait_ge(ph["final"], b - 2)
                        a.activation(sg_s[:, 1 - s, :], bank[3 - s][:, 0:P], ACT.Sigmoid).then_inc(ph["sig_done"], 1)
                block_steps(act, 1, body)
                barrier(act)

            for layer in range(4):
                node_tables(layer)
                [edges0, lambda: aggregate(1), edges2, edges3][layer]()
                if layer == 0:
                    act.wait_ge(POST[0]["s"], 4)
                    a.activation(bn[:, 2, :], bn[:, 1, :], ACT.Sqrt).then_inc(POST[0]["a"], 1)
                    barrier(act)
                else:
                    node_updates(layer)

        @block.vector
        def _(dve):
            v = nc.vector
            steps = [0]

            def link(ins):
                steps[0] += 1
                ins.then_inc(dve_step, 1)
                dve.wait_ge(dve_step, steps[0])

            dve.wait_ge(inputs_in, 32)
            dve.wait_ge(const_ready, 3)
            junk = big[:, 4 * EC:5 * EC]
            link(v.tensor_scalar(blk_next[:, 0:EC], raw_dst[:, 0:EC], 7, None, ALU.arith_shift_right))
            link(v.tensor_scalar(blk_next[0:EP - 1, EC:EC + 1], raw_dst[0:EP - 1, EC:EC + 1], 7, None, ALU.arith_shift_right))
            link(v.memset(blk_floats[:, EC:EC + 1], float(NB + 1)))
            link(v.tensor_copy(blk_floats[:, 0:EC], blk_ids))
            link(v.tensor_copy(blk_floats[0:EP - 1, EC:EC + 1], blk_next[0:EP - 1, EC:EC + 1]))
            dve.drain().then_inc(blocks_ready, 1)
            with dve.Fori(0, NB + 1) as b:
                v.tensor_scalar(junk[0:EP, :], blk_floats[:, 0:EC], iota[0:EP, bass.ds(b, 1)], 0.0, ALU.is_lt, ALU.add,
                                accum_out=cnt[0:EP, bass.ds(b, 1)]).then_inc(blk_count, 1)
                dve.wait_ge(blk_count, b + 1)
            link(v.scalar_tensor_tensor(out=junk[0:EP, :], in0=blk_floats[:, 0:EC], scalar=0.0, in1=blk_floats[:, 1:EC + 1],
                                        op0=ALU.add, op1=ALU.is_gt))
            v.tensor_reduce(cnt[0:EP, NB + 1:NB + 2], junk[0:EP, :], AX.X, ALU.add).then_inc(counts_ready, 1)

            dve.wait_ge(starts_ready, 1)
            link(v.tensor_copy(S[:], bank[0][:, 0:NB + 3]))
            link(v.tensor_copy(Si[:, 0, :], S[:]))
            v.tensor_copy(flag[:], Si[0:1, 0, NB + 1:NB + 2])
            link(v.tensor_scalar(S[:, 0:NB + 1], S[:, 0:NB + 1], float(P - 1), None, ALU.add))
            link(v.tensor_copy(Si[:, 1, 0:NB + 1], S[:, 0:NB + 1]))
            link(v.tensor_scalar(Si[:, :, 0:NB + 1], Si[:, :, 0:NB + 1], 7, None, ALU.arith_shift_right))
            F_, C_, T_, D_, dD, Z_ = (pl[:, q, :] for q in range(6))
            link(v.tensor_copy(F_, Si[:, 0, 0:NB + 1]))
            link(v.tensor_copy(C_, Si[:, 1, 0:NB + 1]))
            link(v.memset(pl[:, 2, :], 0.0))
            link(v.memset(Z_, 0.0))
            link(v.tensor_tensor(D_[:, 0:NB], C_[:, 1:NB + 1], F_[:, 0:NB], ALU.subtract))
            link(v.tensor_tensor_scan(T_[:, 1:NB + 1], D_[:, 0:NB], Z_[:, 0:NB], 0.0, ALU.add, ALU.add))
            link(v.tensor_tensor(D_, F_, T_, ALU.subtract))
            link(v.tensor_tensor(dD[:, 0:NB], D_[:, 1:NB + 1], D_[:, 0:NB], ALU.subtract))
            m3 = big[:, 8 * EC:8 * EC + 2 * CHUNKS * NB].rearrange("p (t c b) -> p t c b", t=2, c=CHUNKS)
            Tb = T_[:, 1:NB + 1].unsqueeze(1).broadcast_to([P, CHUNKS, NB])
            dDb = dD[:, 0:NB].unsqueeze(1).broadcast_to([P, CHUNKS, NB])
            ib = icol[:].unsqueeze(2).broadcast_to([P, CHUNKS, NB])
            link(v.tensor_tensor(m3[:, 0], Tb, ib, ALU.is_le))
            link(v.tensor_tensor(m3[:, 1], m3[:, 0], dDb, ALU.mult))
            link(v.tensor_reduce(it_b[:], m3[:, 0], AX.X, ALU.add))
            link(v.tensor_reduce(it_a[:], m3[:, 1], AX.X, ALU.add))
            link(v.tensor_tensor(it_a[:], it_a[:], icol[:], ALU.add))
            link(v.tensor_scalar(it_a[:], it_a[:], float(ROWS - 1), None, ALU.min))
            link(v.tensor_scalar(S[:, 0:NB + 1], S[:, 0:NB + 1], float(1 - P), None, ALU.add))
            link(v.tensor_copy(it_ai[:], it_a[:]))
            dve.wait_ge(tail_ready, 1)
            junk2 = big[0:64, 5 * EC:5 * EC + NB + 1]
            link(v.tensor_tensor(junk2, S[0:64, 0:NB + 1], ident[0:64, 0:NB + 1], ALU.mult))
            link(v.tensor_reduce(s_f[0:64, 5:6], junk2, AX.X, ALU.add))
            dve.drain().then_inc(blocks_ready, 1)
            dve.drain().then_inc(plan_ready, 1)
            falls = dve.value_load(flag[0:1, 0:1], min_val=0, max_val=E)
            with dve.If(falls == 0):
                dve.nop()
            with dve.Else():
                def tile(t, n):
                    dve.wait_ge(sort_in[0], t * 80 + 80)
                    if not (isinstance(t, int) and t == 0):
                        dve.wait_ge(sort_bin, t * 16)
                    v.scalar_tensor_tensor(out=msg[0:n, 0, 0:n], in0=s_bb[0:n, 0:n], scalar=s_f[0:n, 1:2],
                                           in1=tri[0:n, 0:n], op0=ALU.is_equal, op1=ALU.mult).then_inc(sort_go, 1)
                    v.tensor_scalar(msg[0:64, 1, 0:n], s_bb[0:64, 0:n], iota_p[0:64, 0:1], None,
                                    ALU.is_equal).then_inc(sort_go, 1)
                    dve.wait_ge(sort_go, t * 5 + 2)
                    v.tensor_reduce(s_f[0:n, 3:4], msg[0:n, 0, 0:n], AX.X, ALU.add).then_inc(sort_go, 1)
                    v.tensor_reduce(s_f[0:64, 4:5], msg[0:64, 1, 0:n], AX.X, ALU.add).then_inc(sort_go, 1)
                    dve.wait_ge(sort_go, t * 5 + 4)
                    dve.wait_ge(sort_base, t * 16 + 16)
                    v.tensor_tensor(s_f[0:n, 6:7], s_f[0:n, 3:4], s_f[0:n, 2:3], ALU.add).then_inc(sort_go, 1)
                    dve.wait_ge(sort_go, t * 5 + 5)
                    v.tensor_tensor(s_f[0:64, 5:6], s_f[0:64, 5:6], s_f[0:64, 4:5], ALU.add).then_inc(sort_pos, 1)
                    dve.wait_ge(sort_pos, t + 1)
                    v.tensor_copy(s_i[0:n, 3:4], s_f[0:n, 6:7]).then_inc(sort_rank, 1)
                full = E // P
                tile(0, P)
                with dve.Fori(1, full) as t:
                    tile(t, P)
                tile(full, E - full * P)
            dve.nop()

            dve.wait_ge(weights_in, 16 * N_LOADS)
            dve.wait_ge(meta_T, 1)
            for k, w in enumerate((W0T, WmT, WuT)):
                v.tensor_copy(w[:], bank[7][:, k * P:(k + 1) * P])
            v.tensor_scalar(Wl1[:], Wl1[:], float(MUL ** -0.5), None, ALU.mult)
            v.tensor_scalar(fc1s[:], fc1s[:], float(8 ** -0.5), None, ALU.mult)
            v.tensor_scalar(fc2s[:], fc2s[:], float(SILU_NORM / 8.0), None, ALU.mult)
            link(v.tensor_scalar(Wl2[:], Wl2[:], float(0.25 * (2 * MUL) ** -0.5), None, ALU.mult))
            for rows_, q in ((slice(32, 64), 1), (slice(96, 128), 1), (slice(32, 64), 2)):
                v.tensor_scalar(Wl2[rows_, q, 0:32], Wl2[rows_, q, 0:32], float(3 ** -0.5), None, ALU.mult)

            m_i = big[:, 0:2 * META].bitcast(I32)
            m_w = big[:, 2 * META:3 * META]
            m_f = big[:, 3 * META:6 * META]
            dve.wait_ge(meta_rows, 16 * 3 * CHUNKS)
            link(v.tensor_scalar(it_off[:], it_b[:], float(P), None, ALU.mult))
            v.tensor_copy(m_f[:, 0:META], m_i[:, 0:META])
            v.tensor_copy(m_f[:, 2 * META:3 * META], m_w)
            for c in range(CHUNKS):
                lo = META + c * P
                last = v.tensor_scalar(m_f[:, lo:lo + P], m_i[:, lo:lo + P], it_off[:, c:c + 1], None, ALU.subtract)
            dve.drain().then_inc(meta_rel, 1)
            for q in range(3 * CHUNKS):
                dve.wait_ge(meta_T, q + 2)
                to = (src_it, rel_it, w_it)[q // CHUNKS]
                c = q % CHUNKS
                v.tensor_copy(to[:, c * P:(c + 1) * P], bank[1 + q % 6][:, 0:P]).then_inc(meta_out, 1)
            dve.wait_ge(meta_T, 3 * CHUNKS + 2)
            for half, (lo, hi) in enumerate(((0, 4), (4, CHUNKS))):
                n = (hi - lo) * P
                v.tensor_copy(blk_row[0:1, LEAD + lo * P:LEAD + lo * P + n], bank[0 + half][0:1, 0:n])
                w3 = min(n, META - 3 - lo * P)
                v.tensor_copy(blk_row3[0:1, LEAD + 3 + lo * P:LEAD + 3 + lo * P + w3], bank[0 + half][0:1, 0:w3])
                v.tensor_copy(row_row[0:1, LEAD + lo * P:LEAD + lo * P + n], bank[2 + half][0:1, 0:n])
            barrier(dve)

            def node_tables(layer):
                u = NBT * layer
                with dve.Fori(0, NBT) as b:
                    v.bn_stats(at(bn_raw, b), at(X, b)).then_inc(pre["stat"], 1)
                dve.wait_ge(pre["stat"], NBT + u)
                e_m, o_m, e_v, o_v = (bn_raw[:, :, q] for q in (1, 4, 2, 5))
                link(v.tensor_tensor(ln[:, MEAN, :], e_m, o_m, ALU.add))
                link(v.tensor_tensor(ln[:, HALF, :], e_m, o_m, ALU.subtract))
                link(v.tensor_tensor(ln[:, VAR, :], e_v, o_v, ALU.add))
                link(v.tensor_scalar(ln[:, VAR, :], ln[:, VAR, :], 1.0 / D, EPS, ALU.mult, ALU.add))
                link(v.scalar_tensor_tensor(out=ln[:, HALF, :], in0=ln[:, HALF, :], scalar=0.25, in1=ln[:, HALF, :],
                                            op0=ALU.mult, op1=ALU.mult))
                v.tensor_tensor(ln[:, VAR, :], ln[:, VAR, :], ln[:, HALF, :], ALU.add).then_inc(pre["ln_ready"], 1)
                dve.wait_ge(pre["rstd_ready"], layer + 1)
                link(v.reciprocal(ln[:, RSTD, :], ln[:, RSTD, :]))
                v.scalar_tensor_tensor(out=ln[:, NMR, :], in0=ln[:, MEAN, :], scalar=-0.5, in1=ln[:, RSTD, :],
                                       op0=ALU.mult, op1=ALU.mult).then_inc(pre["ln_ready"], 1)

                def body(b, s, live):
                    if live(0):
                        dve.wait_ge(pre["t_done"], b + (1 + u))
                        if live(2):
                            dve.wait_ge(pre["mm_done"], b + (u - 1))
                        v.tensor_copy(tT[:, s, 0:P], bank[s][:, 0:P]).then_inc(pre["tT_ready"], 1)
                block_steps(dve, 1, body)
                barrier(dve)

            def onehot(ph, n, k, weighted, first, freed):
                if not first:
                    dve.wait_ge(freed, n - RING + 1)
                if weighted:
                    v.tensor_scalar(oh[:, k, :], iota[:], rel_it[:, bass.ds(n, 1)], w_it[:, bass.ds(n, 1)],
                                    ALU.is_equal, ALU.mult).then_inc(ph["oh_ready"], 1)
                else:
                    v.tensor_scalar(oh[:, k, :], iota[:], rel_it[:, bass.ds(n, 1)], None,
                                    ALU.is_equal).then_inc(ph["oh_ready"], 1)

            def accumulate(layer, ph, n, lag, reg, ps):
                b = dve.snap(reg, min_val=0, max_val=NB)
                dve.wait_ge(ph["agg_done"], n - lag + 1)
                if not (isinstance(n, int) and n == lag):
                    dve.wait_ge(ph["acc_done"], n - lag)
                to = at(acc[layer], b)
                v.tensor_tensor(to, ps, to, ALU.add).then_inc(ph["acc_done"], 1)

            def block_regs(layer):
                return [dve.alloc_register(f"ablk{layer}_{k}") for k in range(RING)]

            def aggregate(layer):
                ph, wid, LAG = EDGE[layer], acc[layer].shape[2], 4
                regs = block_regs(layer)

                def top(turn):
                    dve.load(regs, blk_row[0:1, bass.ds(turn + (LEAD - LAG), RING)])

                def body(n, k, turn, live):
                    if live(0):
                        onehot(ph, n, k, layer == 0, isinstance(n, int), ph["agg_done"])
                    if live(LAG):
                        s = (k - LAG) % RING
                        accumulate(layer, ph, n, LAG, regs[k], bank[s % 4][:, 0:wid])
                edge_steps(dve, LAG, top, body)
                barrier(dve)

            def edges0():
                ph = EDGE[0]
                link(v.tensor_scalar(to_spare[:], src_it[:], -1.0, iota_p[:, 0:1], ALU.mult, ALU.add))
                link(v.tensor_scalar(to_spare[:], to_spare[:], float(NBT * P), None, ALU.add))

                def body(n, k, turn, live):
                    if live(0):
                        onehot(ph, n, k, False, isinstance(n, int), ph["t_done"])
                    if live(1):
                        s = (k - 1) % RING
                        dve.wait_ge(attr_in[s], dma_value(16, A_BEFORE[0], turn, k, 1))
                        if live(1 + 4):
                            dve.wait_ge(ph["sum_done"], n - 1 - 3)
                        v.tensor_scalar(same[:, s % 4, :], src_b[:, s, :], src_it[:, bass.ds(n - 1, 1)], None,
                                        ALU.is_equal).then_inc(ph["same_ready"], 1)
                    if live(6):
                        s = (k - 6) % RING
                        dve.wait_ge(ph["sum_done"], n - 6 + 1)
                        if live(6 + RING):
                            dve.wait_ge(scattered[s % COPIES], turn * (16 // COPIES) + 16 * ((k - 6) // COPIES - 1))
                        v.tensor_copy(z_out[:, s, :], bank[4 + s % 2][:, 0:P]).then_inc(ph["out_ready"], 1)
                    if live(1):
                        s = (k - 1) % RING
                        dve.wait_ge(ph["same_ready"], n - 1 + 1)
                        if not (isinstance(n, int) and n == 1):
                            dve.wait_ge(ph["dup_done"], n - 1)
                        v.tensor_tensor_reduce(dup_junk[:], same[:, s % 4, :], tri[:], 1.0, 0.0, ALU.mult, ALU.add,
                                               dup[:, s:s + 1]).then_inc(ph["dup_done"], 1)
                    if live(2):
                        s = (k - 2) % RING
                        dve.wait_ge(ph["dup_done"], n - 2 + 1)
                        v.scalar_tensor_tensor(out=spare[:, s:s + 1], in0=dup[:, s:s + 1], scalar=0.0,
                                               in1=to_spare[:, bass.ds(n - 2, 1)], op0=ALU.is_gt,
                                               op1=ALU.mult).then_inc(ph["spare_done"], 1)
                    if k % GROUP == 1 and (not isinstance(n, int) or 1 < n <= ITEMS + 1):
                        h = ((k - 1) // GROUP - 1) % 2
                        cols = slice(h * GROUP, (h + 1) * GROUP)
                        if not isinstance(n, int) or n > RING:
                            for c in range(COPIES):
                                dve.wait_ge(scattered[c], n * (16 // COPIES) - (16 // COPIES) * 13)
                        dve.wait_ge(ph["spare_done"], n - 1)
                        v.tensor_tensor(idx[:, cols], spare[:, cols], src_it[:, bass.ds(n - GROUP - 1, GROUP)],
                                        ALU.add).then_inc(ph["idx_ready"], 1)
                edge_steps(dve, 6, lambda turn: None, body)
                barrier(dve)

            def edges2():
                ph, LAG = EDGE[2], 12
                regs = block_regs(2)

                def top(turn):
                    dve.load(regs, blk_row[0:1, bass.ds(turn + (LEAD - LAG), RING)])

                def body(n, k, turn, live):
                    if live(0):
                        onehot(ph, n, k, False, isinstance(n, int), ph["agg_done"])
                    if live(4):
                        s = (k - 4) % RING
                        dve.wait_ge(ph["pre_done"], n - 4 + 1)
                        dve.wait_ge(gathered[s], dma_value(16, G_USES, turn, k, 4))
                        if live(4 + 4):
                            dve.wait_ge(ph["sil_done"], n - 4 - 3)
                            dve.wait_ge(ph["sig_done"], n - 4 - 3)
                        v.tensor_tensor(pre_s[:, s % 4, :], bank[2 + s % 2][:, 0:256], G[:, s, :], ALU.add).then_inc(ph["add_done"], 1)
                    if live(6):
                        s = (k - 6) % RING
                        dve.wait_ge(ph["sig_done"], n - 6 + 1)
                        if live(6 + 4):
                            dve.wait_ge(ph["t2_done"], n - 6 - 3)
                        v.tensor_tensor(sil[:, s % 4, :], pre_s[:, s % 4, 0:P], sg[:, s % 8, 0:P], ALU.mult).then_inc(ph["sil_done"], 1)
                    if live(8):
                        s = (k - 8) % RING
                        dve.wait_ge(ph["m_done"], n - 8 + 1)
                        if live(8 + 4):
                            dve.wait_ge(ph["agg_done"], n - 8 - 3)
                        v.tensor_tensor(msg[:, s % 4, 0:P], bank[5][:, 0:P], sg[:, s % 8, P:2 * P], ALU.mult).then_inc(ph["msg_done"], 1)
                    if live(LAG):
                        s = (k - LAG) % RING
                        accumulate(2, ph, n, LAG, regs[k], bank[6 + s % 2][:, 0:P])
                edge_steps(dve, LAG, top, body)
                barrier(dve)

            def edges3():
                ph, LAG = EDGE[3], 8
                regs = block_regs(3)

                def top(turn):
                    dve.load(regs, blk_row[0:1, bass.ds(turn + (LEAD - LAG), RING)])

                def body(n, k, turn, live):
                    if live(0):
                        onehot(ph, n, k, False, isinstance(n, int), ph["agg_done"])
                    if live(4):
                        s = (k - 4) % RING
                        dve.wait_ge(ph["sig_done"], n - 4 + 1)
                        if live(4 + 4):
                            dve.wait_ge(ph["w_done"], n - 4 - 3)
                        v.tensor_tensor(silT[0:64, s % 4, :], bank[(1, 5)[s % 2]][0:64, 0:P], sg[0:64, s % 4, 0:P],
                                        ALU.mult).then_inc(ph["hid_done"], 1)
                    if live(6):
                        s = (k - 6) % RING
                        dve.wait_ge(ph["w_done"], n - 6 + 1)
                        dve.wait_ge(gathered[s], dma_value(16, 2 * G_USES, turn, k, 6))
                        if live(6 + 4):
                            dve.wait_ge(ph["msg_done"], n - 6 - 3)
                        to = pre_s[:, s % 4, :].rearrange("p (c i f) -> p c i f", c=2, f=MUL)
                        w = bank[2 + s % 2][:, 0:P].rearrange("p (c f) -> p c f", f=MUL)
                        v.tensor_tensor(to[:, :, 0, :], w[:, 0:2, :],
                                        G[:, s, 0:MUL].unsqueeze(1).broadcast_to([P, 2, MUL]), ALU.mult)
                        vecs = G[:, s, MUL:P].rearrange("p (i f) -> p i f", f=MUL).unsqueeze(1).broadcast_to([P, 2, 3, MUL])
                        v.tensor_tensor(to[:, :, 1:4, :], w[:, 2:4, :].unsqueeze(2).broadcast_to([P, 2, 3, MUL]),
                                        vecs, ALU.mult).then_inc(ph["prod_done"], 1)
                    if live(LAG):
                        s = (k - LAG) % RING
                        accumulate(3, ph, n, LAG, regs[k], bank[6 + s % 2][:, 0:L3W])
                edge_steps(dve, LAG, top, body)
                barrier(dve)

            def node_updates(layer):
                ph = POST[layer]
                wid = {1: P, 2: 2 * P, 3: 3 * P}[layer]
                if layer == 1:
                    link(v.tensor_copy(deg[:], acc[1][:, :, 128]))
                if layer == 2:
                    link(v.tensor_scalar(deg[:], deg[:], 1.0, None, ALU.max))
                    v.reciprocal(rdeg[:], deg[:]).then_inc(ph["a"], 1)

                def body(b, s, live):
                    if live(0):
                        dve.wait_ge(ph["t_done"], b + 1)
                        if live(2):
                            dve.wait_ge(ph["mm_done"], b - 1)
                        if layer < 3:
                            v.tensor_copy(tT[:, s, 0:wid], bank[s][:, 0:wid]).then_inc(ph["tT_ready"], 1)
                        else:
                            v.tensor_copy(tT[:, s, 0:2 * P], bank[s][:, 0:2 * P])
                            v.tensor_copy(tT[0:64, s, 2 * P:3 * P], bank[s][0:64, 2 * P:3 * P]).then_inc(ph["tT_ready"], 1)
                    if live(1):
                        o = 1 - s
                        xb, ps = at(X, b - 1), bank[2 + o][:, 0:P]
                        dve.wait_ge(ph["mm_done"], b)
                        if layer == 1:
                            v.scalar_tensor_tensor(out=xb, in0=ps, scalar=0.0, in1=xb, op0=ALU.max,
                                                   op1=ALU.add).then_inc(ph["s"], 1)
                            dve.wait_ge(ph["s"], b)
                            dve.wait_ge(ph["h_ready"], b)
                            v.tensor_tensor(xb, xb, hs[:, o, :], ALU.add).then_inc(ph["final"], 1)
                        elif layer == 2:
                            dve.wait_ge(ph["sig_done"], b)
                            v.tensor_tensor(sg_s[:, o, :], ps, sg_s[:, o, :], ALU.mult).then_inc(ph["s"], 1)
                            dve.wait_ge(ph["s"], b)
                            v.tensor_tensor(xb, xb, sg_s[:, o, :], ALU.add).then_inc(ph["final"], 1)
                        else:
                            v.tensor_tensor(xb, xb, ps, ALU.add).then_inc(ph["final"], 1)
                block_steps(dve, 1, body)
                barrier(dve)

            def batch_norm():
                ph = POST[0]
                z = acc[0][:, 0:NB, :]
                sq = big[:, NBT * 128:2 * NBT * 128].rearrange("p (b f) -> p b f", f=128)[:, 0:NB, :]
                wide = lambda a: a.unsqueeze(1).broadcast_to([P, NB, D])
                r0, r1, r2 = (big[:, q * NBT * 128:(q + 1) * NBT * 128] for q in range(3))
                dve.wait_ge(sums_in, 16 * (COPIES - 1))
                link(v.tensor_tensor(r0, r0, r1, ALU.add))
                dve.drain().then_inc(ph["s"], 1)
                link(v.tensor_tensor(r0, r0, r2, ALU.add))
                dve.wait_ge(sums_in, 16 * COPIES)
                v.tensor_tensor(r0, r0, r1, ALU.add).then_inc(ph["s"], 1)
                dve.wait_ge(ph["z"], 1)
                link(v.tensor_scalar(bn[:, 0, :], bank[0][:, 0:P], 1.0 / N, None, ALU.mult))
                link(v.tensor_tensor(z, z, wide(bn[:, 0, :]), ALU.subtract))
                v.tensor_tensor(sq, z, z, ALU.mult).then_inc(ph["s"], 1)
                dve.wait_ge(ph["z"], 2)
                v.tensor_scalar(bn[:, 1, :], bank[1][:, 0:P], 1.0 / N, EPS, ALU.mult, ALU.add).then_inc(ph["s"], 1)
                dve.wait_ge(ph["a"], 1)
                link(v.reciprocal(bn[:, 3, :], bn[:, 2, :]))
                link(v.tensor_tensor(bn[:, 3, :], bn[:, 3, :], gam[:], ALU.mult))
                link(v.tensor_tensor(z, z, wide(bn[:, 3, :]), ALU.mult))
                link(v.tensor_tensor(z, z, wide(bet[:]), ALU.add))
                rows = N - (NB - 1) * P
                v.scalar_tensor_tensor(out=X[:, 0:NB - 1, :], in0=z[:, 0:NB - 1, :], scalar=0.0,
                                       in1=X[:, 0:NB - 1, :], op0=ALU.max, op1=ALU.add)
                v.scalar_tensor_tensor(out=X[0:rows, NB - 1, :], in0=z[0:rows, NB - 1, :], scalar=0.0,
                                       in1=X[0:rows, NB - 1, :], op0=ALU.max, op1=ALU.add)
                barrier(dve)

            for layer in range(4):
                node_tables(layer)
                [edges0, lambda: aggregate(1), edges2, edges3][layer]()
                if layer == 0:
                    batch_norm()
                else:
                    node_updates(layer)


_INS = ["x", "src", "dst", "edge_attr_4", "edge_attr_64", "edge_attr_8", "edge_weight",
        "L0_gnn_W", "L0_gnn_gamma", "L0_gnn_beta", "L1_gnn_W_msg", "L1_gnn_b_msg", "L1_gnn_W_upd", "L1_gnn_b_upd",
        "L2_gnn_w1", "L2_gnn_b1", "L2_gnn_w2", "L2_gnn_b2", "L2_gnn_wg", "L2_gnn_bg", "L2_gnn_wu", "L2_gnn_bu",
        "L3_gnn_w_lin1_s", "L3_gnn_w_lin1_v", "L3_gnn_fc_w1", "L3_gnn_fc_w2", "L3_gnn_w_lin2_s", "L3_gnn_w_lin2_v"]
_OUTS = [((N, D), "float32")]


def kernel(**inputs):
    import numpy as _np
    import concourse.bacc as _bacc
    from concourse import mybir as _mybir
    from concourse.bass_utils import run_bass_kernel_spmd as _run

    nc = _bacc.Bacc("TRN2", target_bir_lowering=False, num_devices=1)
    arrays, args = {}, []
    for name in _INS:
        a = _np.ascontiguousarray(inputs[name])
        arrays[f"in_{name}_dram"] = a
        args.append(nc.dram_tensor(f"in_{name}_dram", a.shape, _mybir.dt.from_np(a.dtype), kind="ExternalInput").ap())
    for i, (shape, dtype) in enumerate(_OUTS):
        dt = _mybir.dt.from_np(_np.dtype(dtype))
        args.append(nc.dram_tensor(f"out_{i}_dram", shape, dt, kind="ExternalOutput").ap())
    gnn_layers(nc, *args)
    r = _run(nc, [arrays], core_ids=[0])
    return r.results[0]["out_0_dram"]
```
